# Optimizing a Trainium2 kernel written in Bass

```python
import numpy as np
import jax
import jax.numpy as jnp

def _softmax(x, axis=-1):
    return jax.nn.softmax(x, axis=axis)

def _gelu(x):
    return jax.nn.gelu(x, approximate=True)

def _silu(x):
    return jax.nn.silu(x)

def _sigmoid(x):
    return jax.nn.sigmoid(x)

def _layernorm(x, axis=-1, eps=1e-05):
    m = jnp.mean(x, axis=axis, keepdims=True)
    v = jnp.var(x, axis=axis, keepdims=True)
    return (x - m) / jnp.sqrt(v + eps)

def _scatter_add(tgt, idx, src, axis=0):
    return tgt.at[idx].add(src)

def _segment_sum(src, seg, n):
    return jax.ops.segment_sum(src, seg, n)
kernel_name = 'mk_adj_preln_d1_adj_r2_14d646'

def setup_inputs(seed: int=0):
    np.random.seed(seed)
    _w = jnp.asarray

    def _rec_inputs():
        import jax
        import jax.numpy as jnp
        _gk = jax.random.key(seed)
        x = -0.0005207 + 1.001 * jax.random.normal(jax.random.fold_in(_gk, 1), (2048, 256), jnp.float32)
        _w = (1.0 + jnp.arange(2048, dtype=jnp.float32)) ** (-0.5)
        _w = _w / _w.mean()
        _pij = jnp.clip(0.00195312 * _w[:, None] * _w[None, :], 0.0, 1.0)
        _a = jax.random.uniform(jax.random.fold_in(_gk, 2), (2048, 2048)) < _pij
        _a = jnp.logical_or(_a, jnp.eye(2048, dtype=bool))
        _af = _a.astype(jnp.float32)
        _af = _af * jax.random.uniform(jax.random.fold_in(_gk, 3), (2048, 2048), jnp.float32, 0.05, 1)
        adj = _af
        return (x, adj)
    x, adj = _rec_inputs()

    def _L0_gnn_setup():
        import jax, jax.numpy as jnp
        import numpy as np
        N, D_IN, D_ATTN, STEPS, P_NUC, TAU = (2048, 256, 64, 2, 0.9, 1.0)
        LN_EPS = 1e-05

        def _xavier(key, shape):
            fan_in, fan_out = (shape[-2], shape[-1])
            lim = np.sqrt(6.0 / (fan_in + fan_out))
            return jax.random.uniform(key, shape, jnp.float32, -lim, lim)

        def _adj_from_feats(Xa, W1, W2, W3):
            Q = Xa @ W1
            K = Xa @ W3
            logits = Q @ W2 @ K.T / TAU
            idx = jnp.argsort(-logits, axis=1)
            vals = jnp.take_along_axis(logits, idx, axis=1)
            csum = jnp.cumsum(jax.nn.softmax(vals, axis=1), axis=1)
            k_i = jnp.sum(csum < P_NUC, axis=1) + 1
            ranks = jnp.arange(logits.shape[1])[None, :]
            keep_sorted = ranks < k_i[:, None]
            inv = jnp.argsort(idx, axis=1)
            keep = jnp.take_along_axis(keep_sorted, inv, axis=1)
            masked = jnp.where(keep, logits, -jnp.inf)
            return jax.nn.softmax(masked, axis=1)
        key = jax.random.key(seed)
        ks = jax.random.split(key, 9)
        return {'X': jax.random.normal(ks[0], (N, D_IN), jnp.float32), 'S': jax.random.uniform(ks[1], (N, N), jnp.float32), 'W1': _xavier(ks[2], (D_IN, D_ATTN)), 'W2': _xavier(ks[3], (D_ATTN, D_ATTN)), 'W3': _xavier(ks[4], (D_IN, D_ATTN)), 'U1': _xavier(ks[5], (STEPS, D_IN, D_IN)), 'U2': _xavier(ks[6], (STEPS, D_IN, D_IN)), 'U3': _xavier(ks[7], (STEPS, D_IN, D_IN)), 'gamma': jnp.ones((D_IN,), jnp.float32), 'beta': jnp.zeros((D_IN,), jnp.float32)}
    _L0_gnn_all = _L0_gnn_setup()
    _L0_gnn_in = {k: v for k, v in _L0_gnn_all.items() if k in ('W1', 'W2', 'W3', 'U1', 'U2', 'U3', 'gamma', 'beta')}
    del _L0_gnn_all
    return {'x': x, 'adj': adj, 'L0_gnn_W1': _L0_gnn_in['W1'], 'L0_gnn_W2': _L0_gnn_in['W2'], 'L0_gnn_W3': _L0_gnn_in['W3'], 'L0_gnn_U1': _L0_gnn_in['U1'], 'L0_gnn_U2': _L0_gnn_in['U2'], 'L0_gnn_U3': _L0_gnn_in['U3'], 'L0_gnn_gamma': _L0_gnn_in['gamma'], 'L0_gnn_beta': _L0_gnn_in['beta']}

def reference(x, adj, L0_gnn_W1, L0_gnn_W2, L0_gnn_W3, L0_gnn_U1, L0_gnn_U2, L0_gnn_U3, L0_gnn_gamma, L0_gnn_beta):
    import jax
    import jax.numpy as jnp

    def _L0_gnn_ref(X, S, W1, W2, W3, U1, U2, U3, gamma, beta):
        import jax, jax.numpy as jnp
        import numpy as np
        N, D_IN, D_ATTN, STEPS, P_NUC, TAU = (2048, 256, 64, 2, 0.9, 1.0)
        LN_EPS = 1e-05

        def _xavier(key, shape):
            fan_in, fan_out = (shape[-2], shape[-1])
            lim = np.sqrt(6.0 / (fan_in + fan_out))
            return jax.random.uniform(key, shape, jnp.float32, -lim, lim)

        def _adj_from_feats(Xa, W1, W2, W3):
            Q = Xa @ W1
            K = Xa @ W3
            logits = Q @ W2 @ K.T / TAU
            idx = jnp.argsort(-logits, axis=1)
            vals = jnp.take_along_axis(logits, idx, axis=1)
            csum = jnp.cumsum(jax.nn.softmax(vals, axis=1), axis=1)
            k_i = jnp.sum(csum < P_NUC, axis=1) + 1
            ranks = jnp.arange(logits.shape[1])[None, :]
            keep_sorted = ranks < k_i[:, None]
            inv = jnp.argsort(idx, axis=1)
            keep = jnp.take_along_axis(keep_sorted, inv, axis=1)
            masked = jnp.where(keep, logits, -jnp.inf)
            return jax.nn.softmax(masked, axis=1)
        n = X.shape[0]
        S = S + jnp.eye(n, dtype=X.dtype)
        Rf = S / jnp.clip(S.sum(axis=1, keepdims=True), 1e-12)
        Rb = S / jnp.clip(S.sum(axis=0), 1e-12)[:, None]
        Xf, Xb, Xa = (X, X, X)
        Z = jnp.zeros_like(X)
        for s in range(STEPS):
            A = _adj_from_feats(Xa, W1, W2, W3)
            Xf = Rf @ Xf
            Xb = Rb @ Xb
            Xa = A @ Xa
            Z = Z + (Xf @ U1[s] + Xb @ U2[s] + Xa @ U3[s])
        Y = X + Z
        mu = Y.mean(axis=-1, keepdims=True)
        var = Y.var(axis=-1, keepdims=True)
        return (Y - mu) / jnp.sqrt(var + LN_EPS) * gamma + beta
    h = jnp.maximum(_layernorm(x, axis=-1), 0.0)
    x = x + _L0_gnn_ref(h, adj, L0_gnn_W1, L0_gnn_W2, L0_gnn_W3, L0_gnn_U1, L0_gnn_U2, L0_gnn_U3, L0_gnn_gamma, L0_gnn_beta)
    return x

_drawn_inputs = setup_inputs


def setup_inputs(seed=0):
    import zlib

    import numpy as np

    out = dict(_drawn_inputs(seed))
    spreads = {'L0_gnn_gamma': (1.0, 0.2), 'L0_gnn_beta': (0.0, 0.1)}
    factors = {}
    for name, (base, spread) in spreads.items():
        noise = np.random.default_rng([zlib.crc32(name.encode()), seed]).standard_normal(out[name].shape)
        drawn = base * np.exp(spread * noise) if base else spread * noise
        out[name] = jnp.asarray(drawn.astype(out[name].dtype))
    for name, factor in factors.items():
        out[name] = (out[name] * factor).astype(out[name].dtype)
    return out
```

```python
import concourse.bass as bass
from concourse import mybir
from contextlib import ExitStack, contextmanager

F32 = mybir.dt.float32
F32R = mybir.dt.float32r
BF16 = mybir.dt.bfloat16
I32 = mybir.dt.int32
ALU = mybir.AluOpType
ACT = mybir.ActivationFunctionType
AX_X = mybir.AxisListType.X
RMAX = bass.bass_isa.ReduceOp.max

P = 128
N = 2048
D = 256
DA = 64
NT = N // P
STEPS = 2
P_NUC = 0.9
LN_EPS = 1e-5
NK = 4
NSEG = 16
ROUNDS = 5
NC = 8 * ROUNDS
BISECT = 44
FIRST_GUESS = (1 / 400, 1 / 700)
AIM = ((4.0, 4.0, 20.0), (0.0, 0.0, 8.0, 20.0))


class Chain:

    def __init__(self, eng, sem, constant):
        self.eng, self.sem, self.constant, self.base, self.n = eng, sem, constant, 0, 0

    def mark(self, ins):
        ins.then_inc(self.sem, 1)
        self.n += 1

    def settle(self):
        self.eng.wait_ge(self.sem, self.base + self.n)

    def step(self, ins):
        self.mark(ins)
        self.settle()

    def settle_apart(self):
        value = self.base + self.n
        if not isinstance(value, int):
            value = self.eng.compute_val(value)
            self.eng.wait_ge(self.constant, 1)
        self.eng.wait_ge(self.sem, value)

    def step_apart(self, ins):
        self.mark(ins)
        self.settle_apart()

    def enter(self, i, per):
        self.total = self.n
        self.base = self.n + i * per
        self.n = 0

    def leave(self, units, per, in_body):
        assert self.n == in_body * per, (self.n, in_body, per)
        self.base, self.n = 0, self.total + units * per


@contextmanager
def every(eng, start, stop, step):
    with eng.Fori(start // step, stop // step) as i:
        yield i * step


def wait(eng, sem, value):
    if not isinstance(value, int) or value > 0:
        eng.wait_ge(sem, value)


def live(u, lag, first=0):
    return not isinstance(u, int) or 0 <= u - lag < NT


def gnn_kernel(nc, x, adj, w1, w2, w3, u1, u2, u3, gamma, beta, out):
    ctx = ExitStack()
    with ctx:
        arena = {"at": -(-nc.sbuf_base // 32) * 32}

        def at(name, shape, dt, offset):
            return nc.alloc_sbuf_tensor_at(name, shape, dt, offset=offset)

        def sb(name, shape, dt=F32):
            size = {F32: 4, F32R: 4, BF16: 2, I32: 4}[dt]
            for d in shape[1:]:
                size *= d
            where = arena["at"]
            arena["at"] += -(-size // 32) * 32
            return at(name, shape, dt, where), where

        def pb(name, shape):
            return ctx.enter_context(nc.psum_tensor(name, shape, F32))

        def sem(name):
            return ctx.enter_context(nc.semaphore(name))

        v_split, o = sb("v_split", [P, NT, 4 * D], F32R)
        h_split = at("h_split", [P, NT, 2 * D], F32R, o)
        colacc = at("colacc", [P, N], F32, o + 10 * 4096)
        y1 = at("y1", [P, NT, D], F32, o + 12 * 4096)
        hy, _ = sb("hy", [P, NT, D])
        xa, o = sb("xa", [P, NT, D])
        x_in = at("x_in", [P, NT, D], F32, o)
        x_again = at("x_again", [P, NT, D], F32, o)
        st_hi, _ = sb("st_hi", [P, 2, NT // 2, P], F32R)
        st_lo, _ = sb("st_lo", [P, 2, NT // 2, P], F32R)
        s_rows, _ = sb("s_rows", [P, 2, N])
        k_hi, _ = sb("k_hi", [P, N], F32R)
        k_lo, _ = sb("k_lo", [P, N], F32R)
        q_both, _ = sb("q_both", [P, N], F32R)
        q_tile, _ = sb("q_tile", [P, 2, P], F32R)
        e, o = sb("e", [P, NK, N])
        u_mats = at("u_mats", [P, 2, 5 * D], F32, o)
        gb = at("gb", [P, 2, D], F32, o)
        squares = at("squares", [P, NT // 2, D], F32, o + 8192)
        win, o = sb("win", [P, N // 2])
        stage = at("stage", [P, 2, 2 * D], F32, o)
        w1_in = at("w1_in", [P, 2, DA], F32, o)
        w2_in = at("w2_in", [DA, DA], F32, o + 512)
        w1_t = at("w1_t", [DA, 2, P], F32, o + 1024)
        junk, o = sb("junk", [P, N], BF16)
        v_tmp = at("v_tmp", [P, 2 * D], F32, o)
        pt, o = sb("pt", [P, 2, 4, P])
        xt_pair = at("xt_pair", [P, 2, 2 * D], F32, o)
        w12, o = sb("w12", [P, 2, P])
        w33, _ = sb("w33", [P, 2, P])
        xt = at("xt", [P, 2, P], F32, o)
        u3_last, _ = sb("u3_last", [P, 2, D])
        ident, _ = sb("ident", [P, P])
        xa_tile, o = sb("xa_tile", [P, 2, D])
        q_round = at("q_round", [P, P], F32R, o)
        cand = [sb(f"cand{i}", [P, NSEG, 8])[0] for i in range(3)]
        top, _ = sb("top", [P, NC])
        csum, _ = sb("csum", [P, NC])
        pick, _ = sb("pick", [P, NC])
        tr, _ = sb("tr", [P, NK, 2])
        lo, _ = sb("lo", [P, NK, 2])
        hi, _ = sb("hi", [P, NK, 2])
        full, _ = sb("full", [P, NK, 2])
        gs, _ = sb("gs", [P, NK, 2])
        neg_max, _ = sb("neg_max", [P, NK])
        tail, _ = sb("tail", [P, NK])
        t_star, _ = sb("t_star", [P, NK])
        target, _ = sb("target", [P, NK])
        flag, _ = sb("flag", [P, NK])
        flag_any, _ = sb("flag_any", [P, NK], I32)
        p_sum, _ = sb("p_sum", [P, NK, 2])
        p_inv, _ = sb("p_inv", [P, NK])
        sc, _ = sb("sc", [P, 24])
        rowsum, _ = sb("rowsum", [P, NT])
        d_f, _ = sb("d_f", [P, NT])
        d_b, _ = sb("d_b", [P, NT])
        mean, _ = sb("mean", [P, NT])
        rstd, _ = sb("rstd", [P, NT])
        power, _ = sb("power", [P, NT // 2])
        ones, _ = sb("ones", [P, 1])
        assert arena["at"] <= nc.sbuf_usable_end if hasattr(nc, "sbuf_usable_end") and isinstance(nc.sbuf_usable_end, int) else True

        lg = pb("lg", [P, N])
        trp = [pb(f"trp{i}", [P, 512]) for i in range(2)]
        acc = pb("acc", [P, 512])
        ms = pb("ms", [P, 512])

        dve_seq, pool_seq = sem("dve_seq"), sem("pool_seq")
        x_loaded = [sem("x_loaded0"), sem("x_loaded1")]
        w_loaded, u_loaded, gb_loaded = sem("w_loaded"), sem("u_loaded"), sem("gb_loaded")
        x_again_loaded, stored = sem("x_again_loaded"), sem("stored")
        s_loaded = [sem("s_loaded0"), sem("s_loaded1")]
        consts_set = sem("consts_set")
        centered, squared, var_set, rstd_set = sem("centered"), sem("squared"), sem("var_set"), sem("rstd_set")
        normed, h_set = sem("normed"), sem("h_set")
        w1t_made, w1t_copied, w12_made, w12_copied = sem("w1t_made"), sem("w1t_copied"), sem("w12_made"), sem("w12_copied")
        staged, staged_t, xt_copied, projected, proj_read = (sem("staged"), sem("staged_t"), sem("xt_copied"),
                                                             sem("projected"), sem("proj_read"))
        v_scaled, v_hi_set, v_done = sem("v_scaled"), sem("v_hi_set"), sem("v_done")
        colsum_made, scales_set = sem("colsum_made"), sem("scales_set")
        diag_done, col_done, row_done = sem("diag_done"), sem("col_done"), sem("row_done")
        h_hi_copied, h_lo_set, y_final, relu_done = sem("h_hi_copied"), sem("h_lo_set"), sem("y_final"), sem("relu_done")
        q_copied, lg_full, max_done, exp_done = sem("q_copied"), sem("lg_full"), sem("max_done"), sem("exp_done")
        guess_set, mass_done = sem("guess_set"), sem("mass_done")
        flag_set, flag_reduced = sem("flag_set"), sem("flag_reduced")
        p_ready, pt_full, pt_copied, ax_done, xa_done = (sem("p_ready"), sem("pt_full"), sem("pt_copied"),
                                                         sem("ax_done"), sem("xa_done"))
        st_full, hi_done, lo_done, st_used, acc_read = (sem("st_full"), sem("hi_done"), sem("lo_done"),
                                                        sem("st_used"), sem("acc_read"))
        post_t, post_xt, post_z, z_read = sem("post_t"), sem("post_xt"), sem("post_z"), sem("z_read")

        block = ctx.enter_context(nc.Block())

        def wait_apart(eng, sem, value):
            if not isinstance(value, int):
                value = eng.compute_val(value)
                eng.wait_ge(consts_set, 1)
            wait(eng, sem, value)

        def run_slots(eng, slot, chain, per, s):
            for u in range(NK):
                slot(s, u, u)
            with every(eng, NK, NT, NK) as u0:
                if chain:
                    chain.enter(u0 - NK, per[s])
                for k in range(NK):
                    slot(s, u0 + k, k)
                if chain:
                    chain.leave(NT - NK, per[s], NK)
            for u in range(NT, NT + NK):
                slot(s, u, u % NK)

        @block.sync
        def _(sp):
            for c in range(2):
                sp.dma_start(x_in[:, 8 * c:8 * c + 8, :],
                             x[c * N // 2:(c + 1) * N // 2, :].rearrange("(t p) d -> p t d", p=P)).then_inc(x_loaded[c], 16)
            sp.dma_start(w1_in[:, :, :], w1.rearrange("(k p) a -> p k a", p=P)).then_inc(w_loaded, 16)
            sp.dma_start(w2_in[:, :], w2).then_inc(w_loaded, 16)
            for c in range(2):
                sp.dma_start(w33[:, :, c * DA:(c + 1) * DA], w3.rearrange("(k p) a -> p k a", p=P)).then_inc(w_loaded, 16)
            sp.dma_start(u3_last[:, :, :], u3[1].rearrange("(k p) d -> p k d", p=P)).then_inc(w_loaded, 16)

            def load_s(g, row, b, sums_read):
                transposed = 4 * (g - 1)
                if not isinstance(transposed, int):
                    transposed = sp.compute_val(transposed)
                wait(sp, st_full, transposed)
                if sums_read is not None:
                    sp.wait_ge(row_done, sums_read)
                    sp.wait_ge(col_done, sums_read)
                sp.dma_start(s_rows[:, b, :], adj[bass.ds(row * P, P), :]).then_inc(s_loaded[b], 16)

            for b in range(2):
                load_s(b, b, b, None)
            with every(sp, 2, NT, 2) as t:
                for b in range(2):
                    load_s(t + b, t + b, b, sp.compute_val(t + b - 1))
            for b in range(2):
                load_s(NT + b, b, b, NT - 1 + b)
            sp.wait_ge(xa_done, NT)
            for m, src in enumerate((u1[0], u2[0], u1[1], u2[1], u3[0])):
                sp.dma_start(u_mats[:, :, m * D:(m + 1) * D], src.rearrange("(k p) d -> p k d", p=P)).then_inc(u_loaded, 16)
            with every(sp, 2, NT, 2) as t:
                for b in range(2):
                    load_s(t + b + NT, t + b, b, None)
            sp.wait_ge(xa_done, 2 * NT)
            sp.dma_start(gb[:, 0, :], gamma.partition_broadcast(P)).then_inc(gb_loaded, 16)
            sp.dma_start(gb[:, 1, :], beta.partition_broadcast(P)).then_inc(gb_loaded, 16)
            sp.dma_start(x_again[:, :, :], x.rearrange("(t p) d -> p t d", p=P)).then_inc(x_again_loaded, 16)
            for c in range(2):
                sp.wait_ge(y_final, c + 1)
                sp.dma_start(out[c * N // 2:(c + 1) * N // 2, :].rearrange("(t p) d -> p t d", p=P),
                             hy[:, 8 * c:8 * c + 8, :]).then_inc(stored, 16)
            sp.wait_ge(stored, 32)

        @block.gpsimd
        def _(pool):
            seq = Chain(pool, pool_seq, consts_set)
            seq.mark(pool.memset(ident[:, :], 0.0))
            seq.mark(pool.memset(power[:, :], -0.5))
            seq.mark(pool.memset(colacc[:, :], 0.0))
            seq.mark(pool.memset(ones[:, :], 1.0))
            seq.mark(pool.memset(full[:, :, :], 1.0001))
            seq.settle()
            pool.affine_select(out=ident[:, :], in_=ident[:, :], compare_op=ALU.not_equal, fill=1.0, base=0,
                               pattern=[[-1, P]], channel_multiplier=1).then_inc(consts_set, 1)
            pool.wait_ge(consts_set, 1)

            def inverse_root(n):
                pool.wait_ge(var_set, n + 1)
                c = n % 2
                pool.tensor_tensor(rstd[:, 8 * c:8 * c + 8], rstd[:, 8 * c:8 * c + 8], power[:, :],
                                   ALU.pow).then_inc(rstd_set, 1)

            inverse_root(0)
            inverse_root(1)

            def stage_tile(ph, t, b):
                n = NT * ph + t
                wait_apart(pool, staged_t, n - 1)
                if ph:
                    pool.tensor_copy(stage[:, b, D:2 * D], y1[:, bass.ds(t, 1), :].rearrange("p a d -> p (a d)"))
                src = xa if ph else hy
                pool.tensor_copy(stage[:, b, 0:D], src[:, bass.ds(t, 1), :].rearrange("p a d -> p (a d)")).then_inc(staged, 1)

            def slot(s, u, k):
                g = NT * s + u
                if live(u, 0):
                    wait_apart(pool, lg_full, g - 1)
                    pool.tensor_copy(q_tile[:, k % 2, :], q_both[:, bass.ds(u * P, P)]).then_inc(q_copied, 1)
                    wait_apart(pool, s_loaded[k % 2], 8 * (g - k % 2) + 16)
                    diag = s_rows[:, k % 2, bass.ds(u * P, P)]
                    pool.tensor_tensor(diag, diag, ident[:, :], ALU.add).then_inc(diag_done, 1)
                    if s == 0:
                        wait_apart(pool, diag_done, g + 1)
                        wait_apart(pool, col_done, g)
                        pool.tensor_tensor(colacc[:, :], colacc[:, :], s_rows[:, k % 2, :], ALU.add).then_inc(col_done, 1)
                if live(u, 2):
                    kk = (k - 2) % NK
                    wait_apart(pool, flag_set, g - 1)
                    pool.partition_all_reduce(flag_any[:, kk:kk + 1], flag[:, kk:kk + 1], P, RMAX).then_inc(flag_reduced, 1)

            for s in range(STEPS):
                if s == 0:
                    pool.wait_ge(h_set, 2)
                    pool.wait_ge(w12_made, 1)
                else:
                    pool.wait_ge(xa_done, NT)
                    pool.wait_ge(acc_read, NT)
                for b in range(2):
                    stage_tile(s, b, b)
                with every(pool, 2, NT, 2) as t:
                    for b in range(2):
                        stage_tile(s, t + b, b)
                pool.wait_ge(proj_read, NT * (s + 1))
                run_slots(pool, slot, None, None, s)
            inverse_root(2)
            inverse_root(3)

        @block.tensor
        def _(pe):
            pe.wait_ge(consts_set, 1)
            pe.wait_ge(w_loaded, 80)
            for b in range(2):
                last = nc.tensor.transpose(ms[0:DA, b * P:(b + 1) * P], w1_in[:, b, :], ident[:, :])
            last.then_inc(w1t_made, 1)
            pe.wait_ge(w1t_copied, 1)
            for b in range(2):
                last = nc.tensor.matmul(acc[:, b * DA:(b + 1) * DA], w1_t[:, b, :], w2_in[:, :], start=True, stop=True)
            last.then_inc(w12_made, 1)
            pe.wait_ge(w12_copied, 1)

            proj = [acc, ms]

            def transposes(ph, t, b):
                n = NT * ph + t
                pe.wait_ge(staged, n + 1)
                wait(pe, xt_copied, n - 1)
                for j in range(4 if ph else 2):
                    last = nc.tensor.transpose(trp[b][:, j * P:(j + 1) * P], stage[:, b, j * P:(j + 1) * P], ident[:, :])
                last.then_inc(staged_t, 1)

            def project(ph, t, b):
                n = NT * ph + t
                pe.wait_ge(xt_copied, n + 1)
                wait(pe, proj_read, n - 1)
                if ph:
                    wait(pe, v_done, t - 1)
                for c, w in ((0, w12), (1, w33)):
                    for j in range(2):
                        last = nc.tensor.matmul(proj[b][:, c * P:(c + 1) * P], w[:, j, :], xt_pair[:, b, j * P:(j + 1) * P],
                                                start=(j == 0), stop=(j == 1))
                if ph:
                    for j in range(2):
                        nc.tensor.matmul(proj[b][:, D:2 * D], xt_pair[:, b, j * P:(j + 1) * P],
                                         u_mats[:, j, 4 * D:5 * D], start=(j == 0), stop=(j == 1))
                    for m in range(2):
                        for j in range(2):
                            last = nc.tensor.matmul(lg[:, (2 * b + m) * 512:(2 * b + m + 1) * 512],
                                                    xt_pair[:, b, D + j * P:D + (j + 1) * P],
                                                    u_mats[:, j, 2 * m * D:2 * (m + 1) * D], start=(j == 0), stop=(j == 1))
                last.then_inc(projected, 1)

            def phase(ph):
                def pair(t):
                    transposes(ph, t + 1, 1)
                    project(ph, t, 0)
                    transposes(ph, t + 2, 0)
                    project(ph, t + 1, 1)

                transposes(ph, 0, 0)
                pair(0)
                with every(pe, 2, NT - 2, 2) as t:
                    pair(t)
                transposes(ph, NT - 1, 1)
                project(ph, NT - 2, 0)
                project(ph, NT - 1, 1)

            def logits(g, k):
                pe.wait_ge(q_copied, g + 1)
                wait(pe, exp_done, g)
                for c in range(4):
                    cols = slice(512 * c, 512 * c + 512)
                    nc.tensor.matmul(lg[:, cols], q_tile[:, k % 2, :], k_hi[:, cols], start=True, stop=False)
                    last = nc.tensor.matmul(lg[:, cols], q_tile[:, k % 2, :], k_lo[:, cols], start=False, stop=True)
                last.then_inc(lg_full, 1)

            def s_transposes(g, k, j):
                if j >= 2:
                    pe.wait_ge(lo_done, 4 * g + j - 1)
                else:
                    wait(pe, lo_done, 4 * g)
                for b in range(4):
                    cols = slice((4 * j + b) * P, (4 * j + b + 1) * P)
                    last = nc.tensor.transpose(trp[j % 2][:, b * P:(b + 1) * P], s_rows[:, k % 2, cols], ident[:, :])
                last.then_inc(st_full, 1)

            def s_products(s, g, half):
                if half == 0:
                    wait(pe, acc_read, g)
                pe.wait_ge(lo_done, 4 * g + 2 * half + 2)
                for b in range(NT // 2):
                    j = half * NT // 2 + b
                    first, end = j == 0, j == NT - 1
                    if s == 0:
                        nc.tensor.matmul(acc[:, :], st_hi[:, half, b, :], h_split[:, j, :], start=first, stop=False)
                        last = nc.tensor.matmul(acc[:, 0:D], st_lo[:, half, b, :], h_split[:, j, 0:D], start=False, stop=end)
                    else:
                        nc.tensor.matmul(acc[:, :], st_hi[:, half, b, :], v_split[:, j, 0:512], start=first, stop=False)
                        nc.tensor.matmul(acc[:, :], st_hi[:, half, b, :], v_split[:, j, 512:1024], start=False, stop=False)
                        last = nc.tensor.matmul(acc[:, :], st_lo[:, half, b, :], v_split[:, j, 0:512], start=False, stop=end)
                last.then_inc(st_used, 1)

            def p_transposes(g, k, j):
                wait(pe, pt_copied, 4 * g + j - 1)
                for b in range(4):
                    cols = slice((4 * j + b) * P, (4 * j + b + 1) * P)
                    last = nc.tensor.transpose(trp[j % 2][:, b * P:(b + 1) * P], e[:, k, cols], ident[:, :])
                last.then_inc(pt_full, 1)

            def ax_products(s, g, j):
                pe.wait_ge(pt_copied, 4 * g + j + 1)
                rhs = xa if s else hy
                for b in range(4):
                    i = 4 * j + b
                    last = nc.tensor.matmul(ms[:, 0:D], pt[:, j % 2, b, :], rhs[:, i, :], start=(i == 0), stop=(i == NT - 1))
                last.then_inc(ax_done, 1)

            def slot(s, u, k):
                g = NT * s + u
                if live(u, 0):
                    pe.wait_ge(diag_done, g + 1)
                    logits(g, k)
                    wait(pe, pt_copied, 4 * (g - 3) if not isinstance(u, int) or u > 3 else 4 * NT * s)
                    s_transposes(g, k, 0)
                    s_transposes(g, k, 1)
                if s and live(u, 4):
                    n = u - 4
                    pe.wait_ge(xa_done, NT + n + 1)
                    for j in range(2):
                        last = nc.tensor.transpose(ms[:, D + j * P:D + (j + 1) * P], xa_tile[:, k % 2, j * P:(j + 1) * P], ident[:, :])
                    last.then_inc(post_t, 1)
                if live(u, 0):
                    s_transposes(g, k, 2)
                    s_transposes(g, k, 3)
                    s_products(s, g, 0)
                if s and live(u, 4):
                    n = u - 4
                    pe.wait_ge(post_xt, n + 1)
                    for j in range(2):
                        last = nc.tensor.matmul(ms[:, 0:D], xt[:, j, :], u3_last[:, j, :], start=(j == 0), stop=(j == 1))
                    last.then_inc(post_z, 1)
                if live(u, 0):
                    s_products(s, g, 1)
                if live(u, 3):
                    a = g - 3
                    kk = (k - 3) % NK
                    pe.wait_ge(p_ready, a + 1)
                    if live(u, 0):
                        pe.wait_ge(lo_done, 4 * g + 4)
                    else:
                        pe.wait_ge(lo_done, 4 * NT * (s + 1))
                    p_transposes(a, kk, 0)
                    p_transposes(a, kk, 1)
                    wait(pe, xa_done, a)
                    if s and live(u, 4):
                        pe.wait_ge(z_read, u - 3)
                    for j in range(4):
                        ax_products(s, a, j)
                        if j < 2:
                            p_transposes(a, kk, j + 2)

            for s in range(STEPS):
                if s:
                    pe.wait_ge(col_done, NT)
                    pe.wait_ge(xa_done, NT)
                    for j in range(NT):
                        last = nc.tensor.matmul(acc[:, j:j + 1], colacc[:, j * P:(j + 1) * P], ones[:, :], start=True, stop=True)
                    last.then_inc(colsum_made, 1)
                    pe.wait_ge(scales_set, 1)
                    pe.wait_ge(u_loaded, 80)
                phase(s)
                pe.wait_ge(proj_read, NT * (s + 1))
                if s:
                    pe.wait_ge(v_done, NT)
                else:
                    pe.wait_ge(h_lo_set, 2)
                run_slots(pe, slot, None, None, s)

        @block.scalar
        def _(act):
            def norm_squares(n, src):
                c = n % 2
                act.wait_ge(centered, n + 1)
                wait(act, var_set, n)
                nc.scalar.activation(squares[:, :, :], src[:, 8 * c:8 * c + 8, :], ACT.Square).then_inc(squared, 1)

            norm_squares(0, x_in)
            norm_squares(1, x_in)
            for c in range(2):
                rows = slice(8 * c, 8 * c + 8)
                act.wait_ge(normed, c + 1)
                nc.scalar.activation(hy[:, rows, :], x_in[:, rows, :], ACT.Relu).then_inc(h_set, 1)
                act.wait_ge(h_set, c + 1)
                nc.scalar.copy(h_split[:, rows, 0:D], hy[:, rows, :]).then_inc(h_hi_copied, 1)
            act.wait_ge(w1t_made, 1)
            nc.scalar.copy(w1_t[:, :, :], ms[0:DA, 0:2 * P]).then_inc(w1t_copied, 1)
            act.wait_ge(w12_made, 1)
            for c in range(2):
                last = nc.scalar.copy(w12[:, :, c * DA:(c + 1) * DA], acc[:, 0:2 * DA].rearrange("p (b a) -> p b a", b=2))
            last.then_inc(w12_copied, 1)

            def copy_xt(ph, t, b):
                n = NT * ph + t
                act.wait_ge(staged_t, n + 1)
                wait(act, projected, n - 1)
                w = (4 if ph else 2) * P
                nc.scalar.copy(xt_pair[:, b, 0:w], trp[b][:, 0:w]).then_inc(xt_copied, 1)

            def scale_v(t, b):
                act.wait_ge(projected, NT + t + 1)
                wait(act, v_done, t)
                m = (2 * b + 1) * 512
                nc.scalar.mul(v_tmp[:, 0:D], lg[:, m:m + D], d_f[:, bass.ds(t, 1)])
                nc.scalar.mul(v_tmp[:, D:2 * D], lg[:, m + D:m + 2 * D], d_b[:, bass.ds(t, 1)]).then_inc(v_scaled, 1)
                act.wait_ge(v_scaled, t + 1)
                nc.scalar.copy(v_split[:, bass.ds(t, 1), 0:2 * D].rearrange("p a d -> p (a d)"), v_tmp[:, :]).then_inc(v_hi_set, 1)

            def copy_hi(g, k, j):
                act.wait_ge(st_full, 4 * g + j + 1)
                if j % 2 == 0:
                    wait(act, st_used, 2 * g - 1 + j // 2)
                b = 4 * (j % 2)
                nc.scalar.copy(st_hi[:, j // 2, b:b + 4, :], trp[j % 2][:, :]).then_inc(hi_done, 1)

            def tail_mass(index, k, free):
                act.wait_ge(guess_set, index)
                wait(act, mass_done, index - 1)
                if free is not None:
                    act.wait_ge(*free)
                nc.scalar.activation(junk[:, :], e[:, k, :], ACT.Relu, bias=tr[:, k, 0:1], scale=-1.0,
                                     accum_out=gs[:, k, 0:1]).then_inc(relu_done, 1)
                act.wait_ge(relu_done, index)
                nc.scalar.activation(junk[:, :], e[:, k, :], ACT.Sign, bias=tr[:, k, 0:1], scale=-1.0,
                                     accum_out=gs[:, k, 1:2]).then_inc(mass_done, 1)

            def slot(s, u, k):
                g = NT * s + u
                if live(u, 0):
                    copy_hi(g, k, 0)
                    copy_hi(g, k, 1)
                if live(u, 1):
                    tail_mass(3 * g - 1, (k - 1) % NK, None)
                if s and live(u, 4):
                    act.wait_ge(post_t, u - 3)
                    wait(act, post_z, u - 4)
                    nc.scalar.copy(xt[:, :, :], ms[:, D:2 * D]).then_inc(post_xt, 1)
                if live(u, 0):
                    copy_hi(g, k, 2)
                    copy_hi(g, k, 3)
                    act.wait_ge(max_done, g + 1)
                    wait(act, pt_full, 4 * (g - 3))
                    nc.scalar.activation(e[:, k, :], lg[:, :], ACT.Exp, bias=neg_max[:, k:k + 1],
                                         accum_out=full[:, k, 1:2]).then_inc(exp_done, 1)
                if live(u, 1):
                    tail_mass(3 * g, (k - 1) % NK, None)
                if live(u, 0):
                    if s == 0:
                        act.wait_ge(diag_done, g + 1)
                        wait(act, mass_done, 3 * g)
                        nc.scalar.activation(junk[:, :], s_rows[:, k % 2, :], ACT.Copy,
                                             accum_out=rowsum[:, bass.ds(u, 1)]).then_inc(row_done, 1)
                    tail_mass(3 * g + 1, k, (v_done, NT) if s else (row_done, g + 1))
                if live(u, 3):
                    a = g - 3
                    kk = (k - 3) % NK
                    for j in range(4):
                        act.wait_ge(pt_full, 4 * a + j + 1)
                        wait(act, ax_done, 4 * a + j - 1)
                        nc.scalar.copy(pt[:, j % 2, :, :], trp[j % 2][:, :]).then_inc(pt_copied, 1)
                    act.wait_ge(ax_done, 4 * a + 4)
                    if s == 0:
                        dst = xa[:, bass.ds(u - 3, 1), :].rearrange("p a d -> p (a d)")
                    else:
                        wait(act, post_t, u - 4)
                        dst = xa_tile[:, kk % 2, :]
                    nc.scalar.mul(dst, ms[:, 0:D], p_inv[:, kk:kk + 1]).then_inc(xa_done, 1)

            for s in range(STEPS):
                if s:
                    act.wait_ge(scales_set, 1)
                    act.wait_ge(mass_done, 3 * NT)
                copy_xt(s, 0, 0)
                with every(act, 0, NT - 2, 2) as t:
                    for b in range(2):
                        copy_xt(s, t + 1 + b, 1 - b)
                        if s:
                            scale_v(t + b, b)
                copy_xt(s, NT - 1, 1)
                if s:
                    scale_v(NT - 2, 0)
                    scale_v(NT - 1, 1)
                run_slots(act, slot, None, None, s)
            norm_squares(2, hy)
            norm_squares(3, hy)

        @block.vector
        def _(dve):
            seq = Chain(dve, dve_seq, consts_set)
            V = nc.vector

            def col(i):
                return sc[:, i:i + 1]

            def normalize(n, src):
                c = n % 2
                rows = slice(8 * c, 8 * c + 8)
                view, m, r = src[:, rows, :], mean[:, rows], rstd[:, rows]
                seq.step(V.tensor_reduce(m, view, AX_X, ALU.add))
                seq.step(V.tensor_scalar(m, m, 1.0 / D, None, ALU.mult))
                V.tensor_tensor(view, view, m.unsqueeze(2).to_broadcast([P, NT // 2, D]),
                                ALU.subtract).then_inc(centered, 1)
                dve.wait_ge(squared, n + 1)
                seq.step(V.tensor_reduce(r, squares[:, :, :], AX_X, ALU.add))
                V.tensor_scalar(r, r, 1.0 / D, LN_EPS, ALU.mult, ALU.add).then_inc(var_set, 1)
                dve.wait_ge(rstd_set, n + 1)
                return V.tensor_tensor(view, view, r.unsqueeze(2).to_broadcast([P, NT // 2, D]), ALU.mult)

            for c in range(2):
                dve.wait_ge(x_loaded[c], 16)
                normalize(c, x_in).then_inc(normed, 1)
            for c in range(2):
                rows = slice(8 * c, 8 * c + 8)
                dve.wait_ge(h_hi_copied, c + 1)
                V.tensor_tensor(h_split[:, rows, D:2 * D], hy[:, rows, :], h_split[:, rows, 0:D].bitcast(F32),
                                ALU.subtract).then_inc(h_lo_set, 1)

            def read_projection(ph, t, b):
                n = NT * ph + t
                dve.wait_ge(projected, n + 1)
                cols = bass.ds(t * P, P)
                q, kk = proj_bank[b][:, 0:P], proj_bank[b][:, P:2 * P]
                seq.mark(V.tensor_copy(q_round[:, :], q))
                seq.mark(V.tensor_copy(k_hi[:, cols], kk))
                seq.mark(V.tensor_copy(q_both[0:DA, cols], q[0:DA, :]))
                seq.settle()
                seq.mark(V.tensor_tensor(q_both[DA:P, cols], q[DA:P, :], q_round[DA:P, :].bitcast(F32), ALU.subtract))
                last = V.tensor_tensor(k_lo[:, cols], kk, k_hi[:, cols].bitcast(F32), ALU.subtract)
                if ph:
                    seq.mark(last)
                    y = hy[:, bass.ds(t, 1), :].rearrange("p a d -> p (a d)")
                    dt = bass.ds(t, 1)
                    seq.step(V.tensor_tensor(y, proj_bank[b][:, D:2 * D], y, ALU.add))
                    m = 2 * b * 512
                    seq.step(V.scalar_tensor_tensor(y, lg[:, m:m + D], d_f[:, dt], y, ALU.mult, ALU.add))
                    last = V.scalar_tensor_tensor(y, lg[:, m + D:m + 2 * D], d_b[:, dt], y, ALU.mult, ALU.add)
                last.then_inc(proj_read, 1)
                if ph:
                    dve.wait_ge(v_hi_set, t + 1)
                    hi_part = v_split[:, bass.ds(t, 1), 0:2 * D].rearrange("p a d -> p (a d)").bitcast(F32)
                    lo_part = v_split[:, bass.ds(t, 1), 2 * D:4 * D].rearrange("p a d -> p (a d)")
                    V.tensor_tensor(lo_part, v_tmp[:, :], hi_part, ALU.subtract).then_inc(v_done, 1)
                dve.wait_ge(proj_read, n + 1)

            def split_lo(g, j):
                dve.wait_ge(hi_done, 4 * g + j + 1)
                b = 4 * (j % 2)
                V.tensor_tensor(st_lo[:, j // 2, b:b + 4, :], trp[j % 2][:, :].rearrange("p (b i) -> p b i", b=4),
                                st_hi[:, j // 2, b:b + 4, :].bitcast(F32), ALU.subtract).then_inc(lo_done, 1)

            def masked_halves(k, threshold, op, sums):
                for h in range(2):
                    part = e[:, k, h * N // 2:(h + 1) * N // 2]
                    yield h, V.scalar_tensor_tensor(win[:, :], part, threshold, part, op, ALU.mult,
                                                    accum_out=sc[:, sums + h:sums + h + 1])

            def next_guess(k, aim, first):
                t, r, big_r = tr[:, k, 0:1], tr[:, k, 1:2], tail[:, k:k + 1]
                pair, lo2, hi2 = tr[:, k, :], lo[:, k, :], hi[:, k, :]
                seq.mark(V.tensor_scalar(col(1), r, big_r, None, ALU.is_le))
                seq.mark(V.tensor_scalar(col(2), r, big_r, 8192.0, ALU.is_le, ALU.mult))
                seq.mark(V.tensor_scalar(col(3), t, aim, big_r, ALU.mult, ALU.add))
                seq.settle()
                if first:
                    seq.mark(V.tensor_scalar(lo2, pair, col(1), None, ALU.mult))
                else:
                    seq.mark(V.scalar_tensor_tensor(lo2, pair, col(1), lo2, ALU.mult, ALU.max))
                seq.mark(V.scalar_tensor_tensor(hi2, pair, col(2), full[:, k, :] if first else hi2, ALU.add, ALU.min))
                seq.settle()
                seq.mark(V.tensor_tensor(sc[:, 4:6], hi2, lo2, ALU.subtract))
                seq.mark(V.tensor_scalar(col(6), col(3), hi[:, k, 1:2], lo[:, k, 1:2], ALU.min, ALU.subtract))
                seq.settle()
                seq.step(V.reciprocal(col(7), col(5)))
                seq.step(V.tensor_scalar(col(8), col(6), col(7), col(4), ALU.mult, ALU.mult))
                return V.tensor_scalar(t, col(8), lo[:, k, 0:1], None, ALU.add)

            def mass_from_sums(g, index, k):
                dve.wait_ge(mass_done, index)
                seq.step(V.tensor_scalar(col(0), gs[:, k, 1:2], 0.5, N / 2, ALU.mult, ALU.add))
                seq.step(V.tensor_scalar(tr[:, k, 1:2], col(0), tr[:, k, 0:1], gs[:, k, 0:1], ALU.mult, ALU.subtract))

            def search_window(s, k):
                for h, ins in masked_halves(k, tr[:, k, 0:1], ALU.is_lt, 10):
                    seq.step_apart(ins)
                    for i in range(NSEG // 2):
                        last = V.max(cand[0][:, h * NSEG // 2 + i, :], win[:, i * P:(i + 1) * P])
                    seq.step(last)
                seq.mark(V.tensor_scalar(col(12), col(10), col(11), -1.0, ALU.add, ALU.mult))
                seq.mark(V.tensor_scalar(target[:, k:k + 1], full[:, k, 1:2], P_NUC, None, ALU.mult))
                seq.mark(V.tensor_reduce(col(14), cand[0][:, :, 7:8].rearrange("p s a -> p (s a)"), AX_X, ALU.max))
                seq.settle_apart()
                src = 0
                for r in range(ROUNDS):
                    eight = top[:, 8 * r:8 * r + 8]
                    seq.mark(V.max(eight, cand[src][:, :, :].rearrange("p s c -> p (s c)")))
                    if r == 0:
                        seq.mark(V.tensor_scalar(col(13), col(12), full[:, k, 1:2], None, ALU.add))
                    seq.settle_apart()
                    if r < ROUNDS - 1:
                        dst = 1 if src != 1 else 2
                        seq.step_apart(V.match_replace(cand[dst][:, :, :].rearrange("p s c -> p (s c)"), eight,
                                                 cand[src][:, :, :].rearrange("p s c -> p (s c)"), 0.0))
                        src = dst
                goal, best = target[:, k:k + 1], t_star[:, k:k + 1]
                seq.step(V.tensor_tensor_scan(csum[:, :], top[:, :], top[:, :], col(13), ALU.add, ALU.max))
                seq.step(V.tensor_scalar(pick[:, :], csum[:, :], goal, None, ALU.is_lt, ALU.add, accum_out=col(15)))
                seq.step(V.scalar_tensor_tensor(pick[:, :], csum[:, :], goal, top[:, :], ALU.is_ge, ALU.mult))
                seq.step(V.tensor_reduce(best, pick[:, :], AX_X, ALU.max))
                seq.mark(V.tensor_scalar(pick[:, :], top[:, :], best, None, ALU.is_ge, ALU.add, accum_out=col(16)))
                seq.step(V.tensor_scalar(col(17), col(13), goal, None, ALU.is_ge))
                seq.step(V.tensor_scalar(col(18), col(15), NC - 1.5, col(17), ALU.is_gt, ALU.add))
                seq.mark(V.tensor_scalar(col(20), col(16), col(15), 1.5, ALU.subtract, ALU.is_gt))
                seq.step(V.tensor_scalar(col(19), col(14), best, col(18), ALU.is_ge, ALU.add))
                V.tensor_scalar(flag[:, k:k + 1], col(19), 2.0, col(20), ALU.mult, ALU.add).then_inc(flag_set, 1)

            def drained(ins):
                V.drain()

            def bisect(k):
                goal, low, high, mid = target[:, k:k + 1], t_star[:, k:k + 1], col(21), col(22)
                drained(V.memset(low, 0.0))
                drained(V.memset(high, 2.0))
                with dve.Fori(0, BISECT) as _:
                    drained(V.tensor_scalar(mid, low, high, 0.5, ALU.add, ALU.mult))
                    for _, ins in masked_halves(k, mid, ALU.is_ge, 10):
                        drained(ins)
                    drained(V.tensor_scalar(col(12), col(10), col(11), goal, ALU.add, ALU.is_ge))
                    drained(V.tensor_scalar(col(13), col(12), 4.0, None, ALU.mult))
                    drained(V.tensor_scalar(low, mid, col(12), low, ALU.mult, ALU.max))
                    drained(V.tensor_scalar(high, mid, col(13), high, ALU.add, ALU.min))

            def mask_by_index(k):
                goal, best = target[:, k:k + 1], t_star[:, k:k + 1]
                for _, ins in masked_halves(k, best, ALU.is_gt, 10):
                    drained(ins)
                drained(V.tensor_scalar(col(12), col(10), col(11), -1.0, ALU.add, ALU.mult))
                drained(V.tensor_scalar(col(13), col(12), goal, best, ALU.add, ALU.add))
                drained(V.memset(col(14), 0.0))
                for h in range(2):
                    part = e[:, k, h * N // 2:(h + 1) * N // 2]
                    drained(V.tensor_scalar(win[:, :], part, best, best, ALU.is_equal, ALU.mult))
                    drained(V.tensor_tensor_scan(win[:, :], win[:, :], win[:, :], col(14), ALU.add, ALU.max))
                    drained(V.tensor_copy(col(14), win[:, N // 2 - 1:N // 2]))
                    drained(V.tensor_scalar(win[:, :], win[:, :], col(13), 1e-30, ALU.is_ge, ALU.mult))
                    drained(V.scalar_tensor_tensor(win[:, :], part, best, win[:, :], ALU.subtract, ALU.is_ge))
                    drained(V.scalar_tensor_tensor(part, part, 1.0, win[:, :], ALU.mult, ALU.mult,
                                                   accum_out=col(15 + h)))
                return V.tensor_scalar(p_sum[:, k, 0:1], col(15), col(16), None, ALU.add)

            def mask(a, k):
                wait_apart(dve, flag_reduced, a + 1)
                worst = V.value_load(flag_any[0:1, k:k + 1], min_val=0, max_val=7)
                with dve.If(worst >= 2):
                    bisect(k)
                with dve.If(worst >= 1):
                    mask_by_index(k).then_inc(dve_seq, 1)
                with dve.Else():
                    seq.mark(V.scalar_tensor_tensor(e[:, k, :], e[:, k, :], t_star[:, k:k + 1], e[:, k, :],
                                                    ALU.is_ge, ALU.mult, accum_out=p_sum[:, k, 0:1]))
                seq.settle()
                V.reciprocal(p_inv[:, k:k + 1], p_sum[:, k, 0:1]).then_inc(p_ready, 1)

            def slot(s, u, k):
                g = NT * s + u
                k1, k2, k3 = (k - 1) % NK, (k - 2) % NK, (k - 3) % NK
                if live(u, 0):
                    split_lo(g, 0)
                    split_lo(g, 1)
                if live(u, 1):
                    mass_from_sums(g - 1, 3 * g - 1, k1)
                    next_guess(k1, AIM[s][1], False).then_inc(guess_set, 1)
                if live(u, 3):
                    mask(g - 3, k3)
                if live(u, 0):
                    dve.wait_ge(lg_full, g + 1)
                    V.tensor_reduce(neg_max[:, k:k + 1], lg[:, :], AX_X, ALU.max, negate=True).then_inc(max_done, 1)
                    split_lo(g, 2)
                    split_lo(g, 3)
                    dve.wait_ge(exp_done, g + 1)
                    seq.mark(V.tensor_scalar(tail[:, k:k + 1], full[:, k, 1:2], 1 - P_NUC, None, ALU.mult))
                    V.tensor_scalar(tr[:, k, 0:1], full[:, k, 1:2], FIRST_GUESS[s], 0.5, ALU.mult, ALU.min).then_inc(guess_set, 1)
                if live(u, 1):
                    mass_from_sums(g - 1, 3 * g, k1)
                    seq.step(next_guess(k1, AIM[s][2], False))
                    if s:
                        for _, ins in masked_halves(k1, tr[:, k1, 0:1], ALU.is_lt, 10):
                            seq.step(ins)
                        seq.step(V.tensor_scalar(tr[:, k1, 1:2], col(10), col(11), None, ALU.add))
                        seq.step(next_guess(k1, AIM[s][3], False))
                if live(u, 2):
                    search_window(s, k2)
                if live(u, 0):
                    dve.wait_ge(st_used, 2 * g + 2)
                    if s == 0:
                        row = y1[:, bass.ds(u, 1), :].rearrange("p a d -> p (a d)")
                        seq.step(V.tensor_copy(row, acc[:, 0:D]))
                        V.tensor_tensor(row, acc[:, D:2 * D], row, ALU.add).then_inc(acc_read, 1)
                    else:
                        y = hy[:, bass.ds(u, 1), :].rearrange("p a d -> p (a d)")
                        du = bass.ds(u, 1)
                        seq.step(V.scalar_tensor_tensor(y, acc[:, 0:D], d_f[:, du], y, ALU.mult, ALU.add))
                        V.scalar_tensor_tensor(y, acc[:, D:2 * D], d_b[:, du], y, ALU.mult, ALU.add).then_inc(acc_read, 1)
                if s and live(u, 4):
                    dve.wait_ge(post_z, u - 3)
                    dve.wait_ge(acc_read, g - 3)
                    y = hy[:, bass.ds(u - 4, 1), :].rearrange("p a d -> p (a d)")
                    V.tensor_tensor(y, ms[:, 0:D], y, ALU.add).then_inc(z_read, 1)
                if live(u, 0):
                    mass_from_sums(g, 3 * g + 1, k)
                    next_guess(k, AIM[s][0], True).then_inc(guess_set, 1)

            proj_bank = [acc, ms]
            per = DVE_PER_SLOT
            for s in range(STEPS):
                if s:
                    dve.wait_ge(colsum_made, 1)
                    dve.wait_ge(row_done, NT)
                    seq.mark(V.tensor_scalar(d_b[:, :], acc[:, 0:NT], 1e-12, None, ALU.max))
                    seq.mark(V.tensor_scalar(d_f[:, :], rowsum[:, :], 1e-12, None, ALU.max))
                    seq.settle()
                    seq.mark(V.reciprocal(d_b[:, :], d_b[:, :]))
                    V.reciprocal(d_f[:, :], d_f[:, :]).then_inc(scales_set, 1)
                    dve.wait_ge(scales_set, 1)
                with every(dve, 0, NT, 2) as t:
                    seq.enter(t, PROJ_PER_TILE[s])
                    for b in range(2):
                        read_projection(s, t + b, b)
                    seq.leave(NT, PROJ_PER_TILE[s], 2)
                run_slots(dve, slot, seq, per, s)

            dve.wait_ge(z_read, NT)
            for c in range(2):
                rows = slice(8 * c, 8 * c + 8)
                view = hy[:, rows, :]
                seq.step(normalize(2 + c, hy))
                if c == 0:
                    dve.wait_ge(gb_loaded, 32)
                    dve.wait_ge(x_again_loaded, 16)
                seq.step(V.tensor_tensor(view, view, gb[:, 0:1, :].to_broadcast([P, NT // 2, D]), ALU.mult))
                seq.step(V.tensor_tensor(view, view, gb[:, 1:2, :].to_broadcast([P, NT // 2, D]), ALU.add))
                V.tensor_tensor(view, view, x_again[:, rows, :], ALU.add).then_inc(y_final, 1)


DVE_PER_SLOT = (63, 76)
PROJ_PER_TILE = (4, 7)

_INS = ["x", "adj", "L0_gnn_W1", "L0_gnn_W2", "L0_gnn_W3", "L0_gnn_U1", "L0_gnn_U2", "L0_gnn_U3", "L0_gnn_gamma",
        "L0_gnn_beta"]


def kernel(**inputs):
    import numpy as _np
    import concourse.bacc as _bacc
    from concourse import mybir as _mybir
    from concourse.bass_utils import run_bass_kernel_spmd as _run

    nc = _bacc.Bacc("TRN2", target_bir_lowering=False, num_devices=1)
    arrays, args = {}, []
    for name in _INS:
        a = _np.ascontiguousarray(inputs[name])
        arrays[f"in_{name}_dram"] = a
        args.append(nc.dram_tensor(f"in_{name}_dram", a.shape, _mybir.dt.from_np(a.dtype), kind="ExternalInput").ap())
    args.append(nc.dram_tensor("out_0_dram", (N, D), _mybir.dt.float32, kind="ExternalOutput").ap())
    gnn_kernel(nc, *args)
    r = _run(nc, [arrays], core_ids=[0])
    return r.results[0]["out_0_dram"]
```
